# Optimizing a Trainium2 kernel written in Bass

```python
import numpy as np
import jax
import jax.numpy as jnp

def _softmax(x, axis=-1):
    return jax.nn.softmax(x, axis=axis)

def _gelu(x):
    return jax.nn.gelu(x, approximate=True)

def _silu(x):
    return jax.nn.silu(x)

def _sigmoid(x):
    return jax.nn.sigmoid(x)

def _layernorm(x, axis=-1, eps=1e-05):
    m = jnp.mean(x, axis=axis, keepdims=True)
    v = jnp.var(x, axis=axis, keepdims=True)
    return (x - m) / jnp.sqrt(v + eps)

def _scatter_add(tgt, idx, src, axis=0):
    return tgt.at[idx].add(src)

def _segment_sum(src, seg, n):
    return jax.ops.segment_sum(src, seg, n)
kernel_name = 'mk_dlrm_tower_d1_rec_r8_0fd68d'

def setup_inputs(seed: int=0):
    np.random.seed(seed)
    _w = jnp.asarray

    def _rec_inputs():
        import jax
        import jax.numpy as jnp
        _tk = jax.random.key(seed)
        dense_ctx = jax.random.normal(jax.random.fold_in(_tk, 190), (512, 16), jnp.float32)
        ids = jnp.stack([jax.random.randint(jax.random.fold_in(_tk, 200 + f), (512,), 0, v, jnp.int32) for f, v in enumerate([1000, 1000, 1000, 12500, 125000, 12500, 12500, 1250, 12500, 12500, 12500, 12500, 12500, 12500, 125000, 1000, 1000, 12500, 1250, 12500, 1250, 12500, 12500, 1250, 12500, 1000, 1000, 1000, 1000, 1000, 12500, 12500])], axis=1)
        tbl_0 = 0.05 * jax.random.normal(jax.random.fold_in(_tk, 500 + 0), (1000, 64), jnp.float32)
        tbl_1 = 0.05 * jax.random.normal(jax.random.fold_in(_tk, 500 + 1), (1000, 64), jnp.float32)
        tbl_2 = 0.05 * jax.random.normal(jax.random.fold_in(_tk, 500 + 2), (1000, 64), jnp.float32)
        tbl_3 = 0.05 * jax.random.normal(jax.random.fold_in(_tk, 500 + 3), (12500, 64), jnp.float32)
        tbl_4 = 0.05 * jax.random.normal(jax.random.fold_in(_tk, 500 + 4), (125000, 64), jnp.float32)
        tbl_5 = 0.05 * jax.random.normal(jax.random.fold_in(_tk, 500 + 5), (12500, 64), jnp.float32)
        tbl_6 = 0.05 * jax.random.normal(jax.random.fold_in(_tk, 500 + 6), (12500, 64), jnp.float32)
        tbl_7 = 0.05 * jax.random.normal(jax.random.fold_in(_tk, 500 + 7), (1250, 64), jnp.float32)
        tbl_8 = 0.05 * jax.random.normal(jax.random.fold_in(_tk, 500 + 8), (12500, 64), jnp.float32)
        tbl_9 = 0.05 * jax.random.normal(jax.random.fold_in(_tk, 500 + 9), (12500, 64), jnp.float32)
        tbl_10 = 0.05 * jax.random.normal(jax.random.fold_in(_tk, 500 + 10), (12500, 64), jnp.float32)
        tbl_11 = 0.05 * jax.random.normal(jax.random.fold_in(_tk, 500 + 11), (12500, 64), jnp.float32)
        tbl_12 = 0.05 * jax.random.normal(jax.random.fold_in(_tk, 500 + 12), (12500, 64), jnp.float32)
        tbl_13 = 0.05 * jax.random.normal(jax.random.fold_in(_tk, 500 + 13), (12500, 64), jnp.float32)
        tbl_14 = 0.05 * jax.random.normal(jax.random.fold_in(_tk, 500 + 14), (125000, 64), jnp.float32)
        tbl_15 = 0.05 * jax.random.normal(jax.random.fold_in(_tk, 500 + 15), (1000, 64), jnp.float32)
        tbl_16 = 0.05 * jax.random.normal(jax.random.fold_in(_tk, 500 + 16), (1000, 64), jnp.float32)
        tbl_17 = 0.05 * jax.random.normal(jax.random.fold_in(_tk, 500 + 17), (12500, 64), jnp.float32)
        tbl_18 = 0.05 * jax.random.normal(jax.random.fold_in(_tk, 500 + 18), (1250, 64), jnp.float32)
        tbl_19 = 0.05 * jax.random.normal(jax.random.fold_in(_tk, 500 + 19), (12500, 64), jnp.float32)
        tbl_20 = 0.05 * jax.random.normal(jax.random.fold_in(_tk, 500 + 20), (1250, 64), jnp.float32)
        tbl_21 = 0.05 * jax.random.normal(jax.random.fold_in(_tk, 500 + 21), (12500, 64), jnp.float32)
        tbl_22 = 0.05 * jax.random.normal(jax.random.fold_in(_tk, 500 + 22), (12500, 64), jnp.float32)
        tbl_23 = 0.05 * jax.random.normal(jax.random.fold_in(_tk, 500 + 23), (1250, 64), jnp.float32)
        tbl_24 = 0.05 * jax.random.normal(jax.random.fold_in(_tk, 500 + 24), (12500, 64), jnp.float32)
        tbl_25 = 0.05 * jax.random.normal(jax.random.fold_in(_tk, 500 + 25), (1000, 64), jnp.float32)
        tbl_26 = 0.05 * jax.random.normal(jax.random.fold_in(_tk, 500 + 26), (1000, 64), jnp.float32)
        tbl_27 = 0.05 * jax.random.normal(jax.random.fold_in(_tk, 500 + 27), (1000, 64), jnp.float32)
        tbl_28 = 0.05 * jax.random.normal(jax.random.fold_in(_tk, 500 + 28), (1000, 64), jnp.float32)
        tbl_29 = 0.05 * jax.random.normal(jax.random.fold_in(_tk, 500 + 29), (1000, 64), jnp.float32)
        tbl_30 = 0.05 * jax.random.normal(jax.random.fold_in(_tk, 500 + 30), (12500, 64), jnp.float32)
        tbl_31 = 0.05 * jax.random.normal(jax.random.fold_in(_tk, 500 + 31), (12500, 64), jnp.float32)
        _rk = jax.random.fold_in(_tk, 7)
        W_top1 = 0.0441942 * jax.random.normal(jax.random.fold_in(_tk, 801), (512, 512), jnp.float32)
        W_top2 = 0.0441942 * jax.random.normal(jax.random.fold_in(_tk, 802), (512, 256), jnp.float32)
        W_top3 = 0.0625 * jax.random.normal(jax.random.fold_in(_tk, 803), (256, 1), jnp.float32)
        b_top1 = jnp.zeros((512,), jnp.float32)
        b_top2 = jnp.zeros((256,), jnp.float32)
        return (dense_ctx, ids, tbl_0, tbl_1, tbl_2, tbl_3, tbl_4, tbl_5, tbl_6, tbl_7, tbl_8, tbl_9, tbl_10, tbl_11, tbl_12, tbl_13, tbl_14, tbl_15, tbl_16, tbl_17, tbl_18, tbl_19, tbl_20, tbl_21, tbl_22, tbl_23, tbl_24, tbl_25, tbl_26, tbl_27, tbl_28, tbl_29, tbl_30, tbl_31, W_top1, b_top1, W_top2, b_top2, W_top3)
    dense_ctx, ids, tbl_0, tbl_1, tbl_2, tbl_3, tbl_4, tbl_5, tbl_6, tbl_7, tbl_8, tbl_9, tbl_10, tbl_11, tbl_12, tbl_13, tbl_14, tbl_15, tbl_16, tbl_17, tbl_18, tbl_19, tbl_20, tbl_21, tbl_22, tbl_23, tbl_24, tbl_25, tbl_26, tbl_27, tbl_28, tbl_29, tbl_30, tbl_31, W_top1, b_top1, W_top2, b_top2, W_top3 = _rec_inputs()

    def _L0_rec_setup():
        import jax, jax.numpy as jnp
        import numpy as np
        B, F, E = (512, 32, 64)
        P = F * (F - 1) // 2
        key = jax.random.key(seed)
        k1, k2 = jax.random.split(key)
        x = jax.random.normal(k1, (B, F, E), dtype=jnp.float32)
        kernel = jax.random.normal(k2, (E, P, E), dtype=jnp.float32) * 0.05
        return {'x': x, 'kernel': kernel}
    _L0_rec_all = _L0_rec_setup()
    _L0_rec_in = {k: v for k, v in _L0_rec_all.items() if k in ('kernel',)}
    del _L0_rec_all
    return {'dense_ctx': dense_ctx, 'ids': ids, 'tbl_0': tbl_0, 'tbl_1': tbl_1, 'tbl_2': tbl_2, 'tbl_3': tbl_3, 'tbl_4': tbl_4, 'tbl_5': tbl_5, 'tbl_6': tbl_6, 'tbl_7': tbl_7, 'tbl_8': tbl_8, 'tbl_9': tbl_9, 'tbl_10': tbl_10, 'tbl_11': tbl_11, 'tbl_12': tbl_12, 'tbl_13': tbl_13, 'tbl_14': tbl_14, 'tbl_15': tbl_15, 'tbl_16': tbl_16, 'tbl_17': tbl_17, 'tbl_18': tbl_18, 'tbl_19': tbl_19, 'tbl_20': tbl_20, 'tbl_21': tbl_21, 'tbl_22': tbl_22, 'tbl_23': tbl_23, 'tbl_24': tbl_24, 'tbl_25': tbl_25, 'tbl_26': tbl_26, 'tbl_27': tbl_27, 'tbl_28': tbl_28, 'tbl_29': tbl_29, 'tbl_30': tbl_30, 'tbl_31': tbl_31, 'W_top1': W_top1, 'b_top1': b_top1, 'W_top2': W_top2, 'b_top2': b_top2, 'W_top3': W_top3, 'L0_rec_kernel': _L0_rec_in['kernel']}

def reference(dense_ctx, ids, tbl_0, tbl_1, tbl_2, tbl_3, tbl_4, tbl_5, tbl_6, tbl_7, tbl_8, tbl_9, tbl_10, tbl_11, tbl_12, tbl_13, tbl_14, tbl_15, tbl_16, tbl_17, tbl_18, tbl_19, tbl_20, tbl_21, tbl_22, tbl_23, tbl_24, tbl_25, tbl_26, tbl_27, tbl_28, tbl_29, tbl_30, tbl_31, W_top1, b_top1, W_top2, b_top2, W_top3, L0_rec_kernel):
    import jax
    import jax.numpy as jnp

    def _L0_rec_ref(x, kernel):
        import jax, jax.numpy as jnp
        import numpy as np
        B, F, E = (512, 32, 64)
        P = F * (F - 1) // 2
        nf = x.shape[1]
        row_idx, col_idx = np.triu_indices(nf, k=1)
        p = x[:, row_idx, :]
        q = x[:, col_idx, :]
        kp = jnp.einsum('bpe,fpe,bpf->bp', p, kernel, q)
        return kp
    e = jnp.stack([tbl_0[ids[:, 0]], tbl_1[ids[:, 1]], tbl_2[ids[:, 2]], tbl_3[ids[:, 3]], tbl_4[ids[:, 4]], tbl_5[ids[:, 5]], tbl_6[ids[:, 6]], tbl_7[ids[:, 7]], tbl_8[ids[:, 8]], tbl_9[ids[:, 9]], tbl_10[ids[:, 10]], tbl_11[ids[:, 11]], tbl_12[ids[:, 12]], tbl_13[ids[:, 13]], tbl_14[ids[:, 14]], tbl_15[ids[:, 15]], tbl_16[ids[:, 16]], tbl_17[ids[:, 17]], tbl_18[ids[:, 18]], tbl_19[ids[:, 19]], tbl_20[ids[:, 20]], tbl_21[ids[:, 21]], tbl_22[ids[:, 22]], tbl_23[ids[:, 23]], tbl_24[ids[:, 24]], tbl_25[ids[:, 25]], tbl_26[ids[:, 26]], tbl_27[ids[:, 27]], tbl_28[ids[:, 28]], tbl_29[ids[:, 29]], tbl_30[ids[:, 30]], tbl_31[ids[:, 31]]], axis=1)
    z = _L0_rec_ref(e, L0_rec_kernel)
    z = z.reshape(z.shape[0], -1)
    h = jnp.concatenate([z, dense_ctx], axis=1)
    h = jnp.maximum(h @ W_top1 + b_top1, 0.0)
    h = jnp.maximum(h @ W_top2 + b_top2, 0.0)
    y = h @ W_top3
    return y

_drawn_inputs = setup_inputs


def setup_inputs(seed=0):
    import zlib

    import numpy as np

    out = dict(_drawn_inputs(seed))
    spreads = {'b_top1': (0.0, 0.1), 'b_top2': (0.0, 0.1)}
    factors = {'tbl_0': 6.746,
     'tbl_1': 5.893,
     'tbl_2': 5.925,
     'tbl_3': 5.853,
     'tbl_4': 5.194,
     'tbl_5': 6.216,
     'tbl_6': 5.859,
     'tbl_7': 5.251,
     'tbl_8': 5.98,
     'tbl_9': 5.444,
     'tbl_10': 5.938,
     'tbl_11': 5.458,
     'tbl_12': 5.264,
     'tbl_13': 5.552,
     'tbl_14': 5.982,
     'tbl_15': 5.631,
     'tbl_16': 5.246,
     'tbl_17': 6.087,
     'tbl_18': 5.357,
     'tbl_19': 5.809,
     'tbl_20': 5.676,
     'tbl_21': 5.964,
     'tbl_22': 6.061,
     'tbl_23': 6.043,
     'tbl_24': 6.093,
     'tbl_25': 5.235,
     'tbl_26': 6.184,
     'tbl_27': 5.743,
     'tbl_28': 6.133,
     'tbl_29': 5.895,
     'tbl_30': 6.028,
     'tbl_31': 6.563}
    for name, (base, spread) in spreads.items():
        noise = np.random.default_rng([zlib.crc32(name.encode()), seed]).standard_normal(out[name].shape)
        drawn = base * np.exp(spread * noise) if base else spread * noise
        out[name] = jnp.asarray(drawn.astype(out[name].dtype))
    for name, factor in factors.items():
        out[name] = (out[name] * factor).astype(out[name].dtype)
    return out
```

```python
import concourse.bass as bass
from concourse import mybir
from contextlib import ExitStack

F32 = mybir.dt.float32
F32R = mybir.dt.float32r
I32 = mybir.dt.int32
MULT = mybir.AluOpType.mult
SUB = mybir.AluOpType.subtract
NOT_EQUAL = mybir.AluOpType.not_equal
COPY = mybir.ActivationFunctionType.Copy
RELU = mybir.ActivationFunctionType.Relu

P = 128
FEATURES, EMB, BATCH = 32, 64, 512
BTILES = BATCH // P
COUPLES = FEATURES // 2
TILES = [(j, m) for j in range(1, FEATURES) for m in range((j + 1) // 2)]
NTILES = len(TILES)
ROUND = 4
ROUNDS = NTILES // ROUND
CHUNK = 16
CHUNKS = NTILES // CHUNK
CHUNK_ROUNDS = CHUNK // ROUND
BLOCK_ROUNDS = P // (2 * ROUND)
BLOCKS = ROUNDS // BLOCK_ROUNDS
STRIP = 32
PAIRS = FEATURES * (FEATURES - 1) // 2
DENSE = 16
H1, H2 = 512, 256
H1T, H2T = H1 // P, H2 // P

X_SLOTS = 3
M_SLOTS = 3
K_SLOTS = 3
PROD_SLOTS = 4


def first_tile(couple):
    return couple * couple


def couple_round(couple):
    if couple == 0:
        return 0
    start, end = first_tile(couple - 1), first_tile(couple)
    return min(end // ROUND, max(-(-start // ROUND) + 1, (end - 12) // ROUND))


def chunk_round(q):
    return max(0, CHUNK_ROUNDS * q - 5)


def z_row(tile, second):
    r = tile // ROUND
    return r // BLOCK_ROUNDS, STRIP * (tile % ROUND) + 2 * (r % BLOCK_ROUNDS) + second


def build(nc, ids, tables, kpairs, dense_t, w1, w1_dense, b1, w2, b2, w3, out):
    couples_at, chunks_at = {}, {}
    for k in range(COUPLES):
        couples_at.setdefault(couple_round(k), []).append(k)
    for q in range(CHUNKS):
        chunks_at.setdefault(chunk_round(q), []).append(q)

    ctx = ExitStack()
    with ctx:
        def sb(name, shape, dt=F32):
            return ctx.enter_context(nc.sbuf_tensor(name, shape, dt))

        def sem(name):
            return ctx.enter_context(nc.semaphore(name))

        ids_sb = sb("ids_sb", [P, BTILES, FEATURES], I32)
        x_rows = sb("x_rows", [P, X_SLOTS, BTILES, 2 * EMB])
        ident = sb("ident", [P, P])
        x_t = sb("x_t", [P, COUPLES, BATCH])
        x_split = sb("x_split", [P, 2, 2, BATCH], F32R)
        moving = sb("moving", [P, M_SLOTS, 2, 2, BATCH], F32R)
        k_raw = sb("k_raw", [P, 2, CHUNK // 2 * P])
        k_split = sb("k_split", [P, 2, 2, CHUNK // 2 * P], F32R)
        k_st = sb("k_st", [P, K_SLOTS, CHUNK, P], F32R)
        prod = sb("prod", [P, PROD_SLOTS, 2, BATCH])
        pick = sb("pick", [P, 2 * STRIP - 2])
        z_t = sb("z_t", [P, BLOCKS, BATCH])
        dense_sb = sb("dense_sb", [DENSE, BATCH])
        w1_sb = sb("w1_sb", [P, BLOCKS, H1])
        w1d_sb = sb("w1d_sb", [DENSE, H1])
        b1_sb = sb("b1_sb", [P, H1T])
        w2_sb = sb("w2_sb", [P, H1T, H2])
        b2_sb = sb("b2_sb", [P, H2T])
        w3_sb = sb("w3_sb", [P, H2T])
        h1_t = sb("h1_t", [P, H1T, BATCH])
        h2_t = sb("h2_t", [P, H2T, BATCH])
        y_sb = sb("y_sb", [1, BATCH])

        bil = ctx.enter_context(nc.psum_tensor("bil", [P, 2, 2, BATCH], F32))
        z_ps = [ctx.enter_context(nc.psum_tensor(f"z_ps{i}", [P, BATCH], F32)) for i in range(2)]
        t_ps = [ctx.enter_context(nc.psum_tensor(f"t_ps{i}", [P, BATCH], F32)) for i in range(2)]

        ids_in = sem("ids_in")
        weights_in = sem("weights_in")
        zeroed = sem("zeroed")
        pick_zeroed = sem("pick_zeroed")
        ident_ready = sem("ident_ready")
        pick_ready = sem("pick_ready")
        gathered = [sem(f"gathered{i}") for i in range(X_SLOTS)]
        transposed = sem("transposed")
        x_high = sem("x_high")
        x_low = sem("x_low")
        moving_ready = sem("moving_ready")
        k_in = [sem(f"k_in{i}") for i in range(2)]
        k_high = sem("k_high")
        k_low = sem("k_low")
        k_placed = [sem(f"k_placed{i}") for i in range(K_SLOTS)]
        bil_done = sem("bil_done")
        prod_done = sem("prod_done")
        summed = sem("summed")
        z_copied = sem("z_copied")
        h1_sum = sem("h1_sum")
        h1_ready = sem("h1_ready")
        h2_sum = sem("h2_sum")
        h2_ready = sem("h2_ready")
        y_sum = sem("y_sum")
        y_ready = sem("y_ready")
        y_out = sem("y_out")

        block = ctx.enter_context(nc.Block())

        @block.gpsimd
        def _(pool):
            pool.wait_ge(zeroed, 1)
            nc.gpsimd.affine_select(out=ident[:, :], in_=ident[:, :], compare_op=NOT_EQUAL, fill=1.0,
                                    base=0, pattern=[[-1, P]], channel_multiplier=1).then_inc(ident_ready, 1)
            pool.wait_ge(ids_in, 16)
            for k in range(COUPLES):
                if k >= X_SLOTS:
                    pool.wait_ge(transposed, k - X_SLOTS + 1)
                for half in range(2):
                    for c in range(BTILES):
                        nc.gpsimd.indirect_dma_start(
                            x_rows[:, k % X_SLOTS, c, half * EMB:(half + 1) * EMB], None, tables[2 * k + half],
                            bass.IndirectOffsetOnAxis(ap=ids_sb[:, c, 2 * k + half:2 * k + half + 1], axis=0),
                        ).then_inc(gathered[k % X_SLOTS], 16)

        @block.sync
        def _(sp):
            sp.dma_start(ids_sb[:, :, :], ids).then_inc(ids_in, 16)
            for q in range(2):
                sp.dma_start(k_raw[:, q, :], kpairs[q, :, :]).then_inc(k_in[q], 16)
            for dst, src in ((dense_sb[:, :], dense_t), (w1_sb[:, :, :], w1), (w1d_sb[:, :], w1_dense),
                             (b1_sb[:, :], b1), (w2_sb[:, :, :], w2), (b2_sb[:, :], b2), (w3_sb[:, :], w3)):
                sp.dma_start(dst, src).then_inc(weights_in, 16)
            half = CHUNK // 2
            for q in range(CHUNKS):
                sp.wait_ge(k_high, q + 1)
                sp.wait_ge(k_low, q + 1)
                if q + 2 < CHUNKS:
                    sp.dma_start(k_raw[:, q % 2, :], kpairs[q + 2, :, :]).then_inc(k_in[q % 2], 16)
                if q >= K_SLOTS:
                    sp.wait_ge(bil_done, (q - K_SLOTS + 1) * CHUNK // 2)
                for tiles in range(2):
                    for part in range(2):
                        sp.dma_start(
                            k_st[part * EMB:(part + 1) * EMB, q % K_SLOTS, tiles * half:(tiles + 1) * half, :].bitcast(F32),
                            k_split[tiles * EMB:(tiles + 1) * EMB, q % 2, part, :].bitcast(F32).rearrange(
                                "p (t n) -> p t n", t=half),
                        ).then_inc(k_placed[q % K_SLOTS], 16)
            sp.wait_ge(y_ready, 1)
            sp.dma_start(out, y_sb[:, :]).then_inc(y_out, 16)
            sp.wait_ge(y_out, 16)

        @block.scalar
        def _(act):
            def split_k(q):
                act.wait_ge(k_in[q % 2], 16 * (q // 2 + 1))
                if q >= 2:
                    act.wait_ge(k_placed[(q - 2) % K_SLOTS], 64 * ((q - 2) // K_SLOTS + 1))
                nc.scalar.activation(k_split[:, q % 2, 0, :], k_raw[:, q % 2, :], COPY).then_inc(k_high, 1)

            def prepare_x(k):
                act.wait_ge(transposed, k + 1)
                s = k % 2
                if k >= 2:
                    act.wait_ge(x_low, k - 1)
                nc.scalar.activation(x_split[:, s, 0, :], t_ps[s][:, :], COPY)
                nc.scalar.activation(x_t[:, k, :], t_ps[s][:, :], COPY).then_inc(x_high, 1)
                if k >= M_SLOTS:
                    act.wait_ge(bil_done, (first_tile(k - M_SLOTS + 1) - 1) // 2 + 1)
                for part in range(2):
                    if part == 0:
                        act.wait_ge(x_high, k + 1)
                    else:
                        act.wait_ge(x_low, k + 1)
                    for feature in range(2):
                        rows = slice(feature * EMB, (feature + 1) * EMB)
                        for copy in range(2):
                            last = nc.scalar.activation(
                                moving[copy * EMB:(copy + 1) * EMB, k % M_SLOTS, feature, part, :],
                                x_split[rows, s, part, :].bitcast(F32), COPY)
                last.then_inc(moving_ready, 1)

            for r in range(ROUNDS):
                for q in chunks_at.get(r, []):
                    split_k(q)
                for k in couples_at.get(r, []):
                    prepare_x(k)
                if r % BLOCK_ROUNDS == 2 and r > 2:
                    g = r // BLOCK_ROUNDS - 1
                    act.wait_ge(summed, BLOCK_ROUNDS * (g + 1))
                    nc.scalar.activation(z_t[:, g, :], z_ps[g % 2][:, :], COPY).then_inc(z_copied, 1)
            act.wait_ge(summed, ROUNDS)
            nc.scalar.activation(z_t[:, BLOCKS - 1, :], z_ps[(BLOCKS - 1) % 2][:, :], COPY).then_inc(z_copied, 1)
            act.wait_ge(weights_in, 16 * 7)
            for n in range(H1T):
                act.wait_ge(h1_sum, n + 1)
                nc.scalar.activation(h1_t[:, n, :], bil[:, n // 2, n % 2, :], RELU,
                                     bias=b1_sb[:, n:n + 1]).then_inc(h1_ready, 1)
            for n in range(H2T):
                act.wait_ge(h2_sum, n + 1)
                nc.scalar.activation(h2_t[:, n, :], t_ps[n][:, :], RELU, bias=b2_sb[:, n:n + 1]).then_inc(h2_ready, 1)
            act.wait_ge(y_sum, 1)
            nc.scalar.activation(y_sb[:, :], z_ps[0][0:1, :], COPY).then_inc(y_ready, 1)

        @block.vector
        def _(dve):
            nc.vector.memset(ident[:, :], 0.0).then_inc(zeroed, 1)
            nc.vector.memset(pick[:, :], 0.0).then_inc(pick_zeroed, 1)
            dve.wait_ge(pick_zeroed, 1)
            nc.vector.memset(pick[0:EMB, STRIP - 2:STRIP - 1], 1.0)
            nc.vector.memset(pick[EMB:P, STRIP - 1:STRIP], 1.0).then_inc(pick_ready, 1)

            def split_k(q):
                dve.wait_ge(k_high, q + 1)
                nc.vector.tensor_tensor(k_split[:, q % 2, 1, :], k_raw[:, q % 2, :],
                                        k_split[:, q % 2, 0, :].bitcast(F32), SUB).then_inc(k_low, 1)

            def split_x(k):
                s = k % 2
                dve.wait_ge(x_high, k + 1)
                if k >= 2:
                    dve.wait_ge(moving_ready, k - 1)
                nc.vector.tensor_tensor(x_split[:, s, 1, :], x_t[:, k, :],
                                        x_split[:, s, 0, :].bitcast(F32), SUB).then_inc(x_low, 1)

            def multiply(g):
                dve.wait_ge(bil_done, g + 1)
                if g >= PROD_SLOTS:
                    dve.wait_ge(summed, (g - PROD_SLOTS) // 2 + 1)
                ma, mb = TILES[2 * g][1], TILES[2 * g + 1][1]
                if mb == ma + 1:
                    nc.vector.tensor_tensor(prod[:, g % PROD_SLOTS, :, :], bil[:, g % 2, :, :],
                                            x_t[:, ma:ma + 2, :], MULT).then_inc(prod_done, 1)
                else:
                    nc.vector.tensor_tensor(prod[:, g % PROD_SLOTS, 0, :], bil[:, g % 2, 0, :],
                                            x_t[:, ma, :], MULT)
                    nc.vector.tensor_tensor(prod[:, g % PROD_SLOTS, 1, :], bil[:, g % 2, 1, :],
                                            x_t[:, mb, :], MULT).then_inc(prod_done, 1)

            for r in range(ROUNDS):
                for q in chunks_at.get(r, []):
                    split_k(q)
                early = [k for k in couples_at.get(r, []) if first_tile(k) // ROUND <= r]
                for k in early:
                    split_x(k)
                multiply(2 * r)
                for k in couples_at.get(r, []):
                    if k not in early:
                        split_x(k)
                multiply(2 * r + 1)

        @block.tensor
        def _(pe):
            def transpose(k):
                slot = k % X_SLOTS
                pe.wait_ge(gathered[slot], 16 * 2 * BTILES * (k // X_SLOTS + 1))
                if k >= 2:
                    pe.wait_ge(x_high, k - 1)
                for c in range(BTILES):
                    last = nc.tensor.transpose(t_ps[k % 2][:, c * P:(c + 1) * P], x_rows[:, slot, c, :], ident[:, :])
                last.then_inc(transposed, 1)

            def contract(g):
                if g >= 2:
                    pe.wait_ge(prod_done, g - 1)
                for t in range(2):
                    tile = 2 * g + t
                    j = TILES[tile][0]
                    for part in range(2):
                        last = nc.tensor.matmul(
                            bil[:, g % 2, t, :], k_st[:, tile // CHUNK % K_SLOTS, tile % CHUNK, :],
                            moving[:, j // 2 % M_SLOTS, j % 2, part, :], start=(part == 0), stop=(part == 1))
                last.then_inc(bil_done, 1)

            def sum_round(r):
                g, s = r // BLOCK_ROUNDS, r % BLOCK_ROUNDS
                pe.wait_ge(prod_done, 2 * r + 2)
                if s == 0 and g >= 2:
                    pe.wait_ge(z_copied, g - 1)
                for c in range(ROUND):
                    last = nc.tensor.matmul(
                        z_ps[g % 2][c * STRIP:(c + 1) * STRIP, :],
                        pick[:, STRIP - 2 - 2 * s:2 * STRIP - 2 - 2 * s],
                        prod[:, (2 * r + c // 2) % PROD_SLOTS, c % 2, :],
                        start=(s == 0), stop=(s == BLOCK_ROUNDS - 1), tile_position=(0, c * STRIP))
                last.then_inc(summed, 1)

            pe.wait_ge(ident_ready, 1)
            pe.wait_ge(pick_ready, 1)
            ready = 0
            for r in range(ROUNDS):
                for k in couples_at.get(r, []):
                    transpose(k)
                if r % CHUNK_ROUNDS == 0:
                    q = r // CHUNK_ROUNDS
                    pe.wait_ge(k_placed[q % K_SLOTS], 64 * (q // K_SLOTS + 1))
                for g in (2 * r, 2 * r + 1):
                    need = max(TILES[2 * g][0], TILES[2 * g + 1][0]) // 2 + 1
                    if need > ready:
                        pe.wait_ge(moving_ready, need)
                        ready = need
                    contract(g)
                if r >= 1:
                    sum_round(r - 1)
            sum_round(ROUNDS - 1)

            pe.wait_ge(weights_in, 16 * 7)
            pe.wait_ge(z_copied, BLOCKS - 1)
            for n in range(H1T):
                cols = slice(n * P, (n + 1) * P)
                nc.tensor.matmul(bil[:, n // 2, n % 2, :], w1d_sb[:, cols], dense_sb[:, :], start=True, stop=False)
                for g in range(BLOCKS - 1):
                    nc.tensor.matmul(bil[:, n // 2, n % 2, :], w1_sb[:, g, cols], z_t[:, g, :], start=False, stop=False)
            pe.wait_ge(z_copied, BLOCKS)
            for n in range(H1T):
                nc.tensor.matmul(bil[:, n // 2, n % 2, :], w1_sb[:, BLOCKS - 1, n * P:(n + 1) * P],
                                 z_t[:, BLOCKS - 1, :], start=False, stop=True).then_inc(h1_sum, 1)
            for n in range(H1T):
                pe.wait_ge(h1_ready, n + 1)
                for m in range(H2T):
                    last = nc.tensor.matmul(t_ps[m][:, :], w2_sb[:, n, m * P:(m + 1) * P], h1_t[:, n, :],
                                            start=(n == 0), stop=(n == H1T - 1))
                    if n == H1T - 1:
                        last.then_inc(h2_sum, 1)
            for m in range(H2T):
                pe.wait_ge(h2_ready, m + 1)
                last = nc.tensor.matmul(z_ps[0][0:1, :], w3_sb[:, m:m + 1], h2_t[:, m, :],
                                        start=(m == 0), stop=(m == H2T - 1))
            last.then_inc(y_sum, 1)


def kernel(**inputs):
    import numpy as np
    import concourse.bacc as bacc
    from concourse.bass_utils import run_bass_kernel_spmd

    first, second = np.triu_indices(FEATURES, k=1)
    pair_of = {(int(i), int(j)): n for n, (i, j) in enumerate(zip(first, second))}
    order = [pair_of.get((2 * m + h, j), PAIRS) for j, m in TILES for h in range(2)]

    weight = np.asarray(inputs["L0_rec_kernel"])
    padded = np.concatenate([weight, np.zeros((EMB, 1, EMB), weight.dtype)], axis=1)[:, order, :]
    kpairs = padded.reshape(EMB, CHUNKS, 2, CHUNK // 2 * P).transpose(1, 2, 0, 3).reshape(
        CHUNKS, P, CHUNK // 2 * P)

    w1 = np.asarray(inputs["W_top1"])
    row_of = np.full((BLOCKS, P), PAIRS)
    for t, (j, m) in enumerate(TILES):
        for h in range(2):
            row_of[z_row(t, h)] = pair_of.get((2 * m + h, j), PAIRS)
    w1_rows = np.concatenate([w1[:PAIRS], np.zeros((1, H1), w1.dtype)], axis=0)[row_of]

    ids = np.asarray(inputs["ids"]).reshape(BTILES, P, FEATURES).transpose(1, 0, 2)
    arrays = {
        "ids": ids,
        **{f"tbl_{n}": np.asarray(inputs[f"tbl_{n}"]) for n in range(FEATURES)},
        "kpairs": kpairs,
        "dense_t": np.asarray(inputs["dense_ctx"]).T,
        "w1": w1_rows.transpose(1, 0, 2),
        "w1_dense": w1[PAIRS:],
        "b1": np.asarray(inputs["b_top1"]).reshape(H1T, P).T,
        "w2": np.asarray(inputs["W_top2"]).reshape(H1T, P, H2).transpose(1, 0, 2),
        "b2": np.asarray(inputs["b_top2"]).reshape(H2T, P).T,
        "w3": np.asarray(inputs["W_top3"]).reshape(H2T, P).T,
    }
    nc = bacc.Bacc("TRN2", target_bir_lowering=False, num_devices=1)
    aps = {}
    for name in list(arrays):
        array = np.ascontiguousarray(arrays.pop(name))
        arrays[name + "_dram"] = array
        aps[name] = nc.dram_tensor(name + "_dram", array.shape, mybir.dt.from_np(array.dtype),
                                   kind="ExternalInput").ap()
    out = nc.dram_tensor("out_dram", (BATCH, 1), F32, kind="ExternalOutput").ap()
    build(nc, aps["ids"], [aps[f"tbl_{n}"] for n in range(FEATURES)], aps["kpairs"], aps["dense_t"], aps["w1"],
          aps["w1_dense"], aps["b1"], aps["w2"], aps["b2"], aps["w3"], out.rearrange("b o -> o b"))
    result = run_bass_kernel_spmd(nc, [arrays], core_ids=[0])
    return result.results[0]["out_dram"]
```

```python
import concourse.bass as bass
from concourse import mybir
from contextlib import ExitStack

F32 = mybir.dt.float32
F32R = mybir.dt.float32r
I32 = mybir.dt.int32
MULT = mybir.AluOpType.mult
ADD = mybir.AluOpType.add
SUB = mybir.AluOpType.subtract
NOT_EQUAL = mybir.AluOpType.not_equal
COPY = mybir.ActivationFunctionType.Copy
RELU = mybir.ActivationFunctionType.Relu

P = 128
FEATURES, EMB, BATCH = 32, 64, 512
BTILES = BATCH // P
COUPLES = FEATURES // 2
TILES = [(j, m) for j in range(1, FEATURES) for m in range((j + 1) // 2)]
NTILES = len(TILES)
ROUND = 4
ROUNDS = NTILES // ROUND
CHUNK = 16
CHUNKS = NTILES // CHUNK
CHUNK_ROUNDS = CHUNK // ROUND
BLOCK_ROUNDS = P // (2 * ROUND)
BLOCKS = ROUNDS // BLOCK_ROUNDS
STRIP = 32
PAIRS = FEATURES * (FEATURES - 1) // 2
DENSE = 16
H1, H2 = 512, 256
H1T, H2T = H1 // P, H2 // P

X_SLOTS = 3
M_SLOTS = 3
K_SLOTS = 3
PROD_SLOTS = 5
BIL_SLOTS = 3


def first_tile(couple):
    return couple * couple


def couple_round(couple):
    if couple == 0:
        return 0
    start, end = first_tile(couple - 1), first_tile(couple)
    return min(end // ROUND, max(-(-start // ROUND) + 1, (end - 12) // ROUND))


def chunk_round(q):
    return max(0, CHUNK_ROUNDS * q - 5)


def high_round(q):
    return max(0, chunk_round(q) - 3)


def z_row(tile, second):
    r = tile // ROUND
    return r // BLOCK_ROUNDS, STRIP * (tile % ROUND) + 2 * (r % BLOCK_ROUNDS) + second


def build(nc, ids, tables, kpairs, dense_rows, w1, b1, w2, b2, w3, out):
    couples_at, chunks_at, high_at = {}, {}, {}
    for k in range(COUPLES):
        couples_at.setdefault(couple_round(k), []).append(k)
    for q in range(CHUNKS):
        chunks_at.setdefault(chunk_round(q), []).append(q)
        high_at.setdefault(high_round(q), []).append(q)

    ctx = ExitStack()
    with ctx:
        def sb(name, shape, dt=F32):
            return ctx.enter_context(nc.sbuf_tensor(name, shape, dt))

        def sem(name):
            return ctx.enter_context(nc.semaphore(name))

        ids_sb = sb("ids_sb", [P, BTILES, FEATURES], I32)
        x_rows = sb("x_rows", [P, X_SLOTS, BTILES, 2 * EMB])
        ident = sb("ident", [P, P])
        x_t = sb("x_t", [P, COUPLES, BATCH])
        x_split = sb("x_split", [P, 2, 2, BATCH], F32R)
        moving = sb("moving", [P, M_SLOTS, 2, 2, BATCH], F32R)
        k_raw = sb("k_raw", [P, 2, CHUNK // 2 * P])
        k_split = sb("k_split", [P, 2, 2, CHUNK // 2 * P], F32R)
        k_st = sb("k_st", [P, K_SLOTS, CHUNK, P], F32R)
        prod = sb("prod", [P, PROD_SLOTS, 2, BATCH])
        pick = sb("pick", [P, 2 * STRIP - 2])
        z_t = sb("z_t", [P, BLOCKS, BATCH])
        dense_sb = sb("dense_sb", [P, BLOCKS, BATCH])
        w1_sb = sb("w1_sb", [P, BLOCKS, H1])
        b1_sb = sb("b1_sb", [P, H1T])
        w2_sb = sb("w2_sb", [P, H1T, H2])
        b2_sb = sb("b2_sb", [P, H2T])
        w3_sb = sb("w3_sb", [P, H2T])
        h1_t = sb("h1_t", [P, H1T, BATCH])
        h2_t = sb("h2_t", [P, H2T, BATCH])
        y_sb = sb("y_sb", [1, BATCH])

        bil = ctx.enter_context(nc.psum_tensor("bil", [P, BIL_SLOTS, 2, BATCH], F32))
        z_ps = ctx.enter_context(nc.psum_tensor("z_ps", [P, BATCH], F32))
        t_ps = ctx.enter_context(nc.psum_tensor("t_ps", [P, BATCH], F32))

        ids_in = sem("ids_in")
        weights_in = sem("weights_in")
        zeroed = sem("zeroed")
        pick_zeroed = sem("pick_zeroed")
        ident_ready = sem("ident_ready")
        pick_ready = sem("pick_ready")
        gathered = [sem(f"gathered{i}") for i in range(X_SLOTS)]
        transposed = sem("transposed")
        x_high = sem("x_high")
        x_ready = sem("x_ready")
        x_low = sem("x_low")
        moving_ready = sem("moving_ready")
        k_in = [sem(f"k_in{i}") for i in range(2)]
        k_high = sem("k_high")
        k_low = sem("k_low")
        k_placed = [sem(f"k_placed{i}") for i in range(K_SLOTS)]
        bil_done = sem("bil_done")
        prod_done = sem("prod_done")
        summed = sem("summed")
        z_copied = sem("z_copied")
        h1_sum = sem("h1_sum")
        h1_ready = sem("h1_ready")
        h2_sum = sem("h2_sum")
        h2_ready = sem("h2_ready")
        y_sum = sem("y_sum")
        y_ready = sem("y_ready")
        y_out = sem("y_out")

        block = ctx.enter_context(nc.Block())

        @block.gpsimd
        def _(pool):
            pool.wait_ge(zeroed, 1)
            nc.gpsimd.affine_select(out=ident[:, :], in_=ident[:, :], compare_op=NOT_EQUAL, fill=1.0,
                                    base=0, pattern=[[-1, P]], channel_multiplier=1).then_inc(ident_ready, 1)
            pool.wait_ge(ids_in, 16)
            for k in range(COUPLES):
                if k >= X_SLOTS:
                    pool.wait_ge(transposed, k - X_SLOTS + 1)
                for half in range(2):
                    for c in range(BTILES):
                        nc.gpsimd.indirect_dma_start(
                            x_rows[:, k % X_SLOTS, c, half * EMB:(half + 1) * EMB], None, tables[2 * k + half],
                            bass.IndirectOffsetOnAxis(ap=ids_sb[:, c, 2 * k + half:2 * k + half + 1], axis=0),
                        ).then_inc(gathered[k % X_SLOTS], 16)

        @block.sync
        def _(sp):
            sp.dma_start(ids_sb[:, :, :], ids).then_inc(ids_in, 16)
            for q in range(2):
                sp.dma_start(k_raw[:, q, :], kpairs[q, :, :]).then_inc(k_in[q], 16)
            for dst, src in ((dense_sb[:, :, :], dense_rows), (w1_sb[:, :, :], w1),
                             (b1_sb[:, :], b1), (w2_sb[:, :, :], w2), (b2_sb[:, :], b2), (w3_sb[:, :], w3)):
                sp.dma_start(dst, src).then_inc(weights_in, 16)
            half = CHUNK // 2
            for q in range(CHUNKS):
                sp.wait_ge(k_high, q + 1)
                sp.wait_ge(k_low, q + 1)
                if q + 2 < CHUNKS:
                    sp.dma_start(k_raw[:, q % 2, :], kpairs[q + 2, :, :]).then_inc(k_in[q % 2], 16)
                if q >= K_SLOTS:
                    sp.wait_ge(bil_done, (q - K_SLOTS + 1) * CHUNK // 2)
                for tiles in range(2):
                    for part in range(2):
                        sp.dma_start(
                            k_st[part * EMB:(part + 1) * EMB, q % K_SLOTS, tiles * half:(tiles + 1) * half, :].bitcast(F32),
                            k_split[tiles * EMB:(tiles + 1) * EMB, q % 2, part, :].bitcast(F32).rearrange(
                                "p (t n) -> p t n", t=half),
                        ).then_inc(k_placed[q % K_SLOTS], 16)
            sp.wait_ge(y_ready, 1)
            sp.dma_start(out, y_sb[:, :]).then_inc(y_out, 16)
            sp.wait_ge(y_out, 16)

        @block.scalar
        def _(act):
            def split_k(q):
                act.wait_ge(k_in[q % 2], 16 * (q // 2 + 1))
                if q >= 2:
                    act.wait_ge(k_placed[(q - 2) % K_SLOTS], 64 * ((q - 2) // K_SLOTS + 1))
                nc.scalar.activation(k_split[:, q % 2, 0, :], k_raw[:, q % 2, :], COPY).then_inc(k_high, 1)

            def prepare_x(k):
                act.wait_ge(transposed, k + 1)
                s = k % 2
                if k >= 2:
                    act.wait_ge(x_low, k - 1)
                nc.scalar.activation(x_split[:, s, 0, :], t_ps[:, :], COPY).then_inc(x_high, 1)
                if k >= M_SLOTS:
                    act.wait_ge(bil_done, (first_tile(k - M_SLOTS + 1) - 1) // 2 + 1)
                for feature in range(2):
                    rows = slice(feature * EMB, (feature + 1) * EMB)
                    for part in range(2):
                        if part == 0:
                            act.wait_ge(x_high, k + 1)
                        else:
                            act.wait_ge(x_low, k + 1)
                        for copy in range(2):
                            last = nc.scalar.activation(
                                moving[copy * EMB:(copy + 1) * EMB, k % M_SLOTS, feature, part, :],
                                x_split[rows, s, part, :].bitcast(F32), COPY)
                    last.then_inc(moving_ready, 1)
                    if feature == 0:
                        nc.scalar.activation(x_t[:, k, :], t_ps[:, :], COPY).then_inc(x_ready, 1)

            for r in range(ROUNDS):
                for q in high_at.get(r, []):
                    split_k(q)
                for k in couples_at.get(r, []):
                    prepare_x(k)
            act.wait_ge(weights_in, 16 * 6)
            for n in range(H1T):
                act.wait_ge(h1_sum, n + 1)
                nc.scalar.activation(h1_t[:, n, :], bil[:, n // 2, n % 2, :], RELU,
                                     bias=b1_sb[:, n:n + 1]).then_inc(h1_ready, 1)
            for n in range(H2T):
                act.wait_ge(h2_sum, n + 1)
                nc.scalar.activation(h2_t[:, n, :], bil[:, 2, n, :], RELU, bias=b2_sb[:, n:n + 1]).then_inc(h2_ready, 1)
            act.wait_ge(y_sum, 1)
            nc.scalar.activation(y_sb[:, :], t_ps[0:1, :], COPY).then_inc(y_ready, 1)

        @block.vector
        def _(dve):
            nc.vector.memset(ident[:, :], 0.0).then_inc(zeroed, 1)
            nc.vector.memset(pick[:, :], 0.0).then_inc(pick_zeroed, 1)
            dve.wait_ge(pick_zeroed, 1)
            nc.vector.memset(pick[0:EMB, STRIP - 2:STRIP - 1], 1.0)
            nc.vector.memset(pick[EMB:P, STRIP - 1:STRIP], 1.0).then_inc(pick_ready, 1)

            def split_k(q):
                dve.wait_ge(k_high, q + 1)
                nc.vector.tensor_tensor(k_split[:, q % 2, 1, :], k_raw[:, q % 2, :],
                                        k_split[:, q % 2, 0, :].bitcast(F32), SUB).then_inc(k_low, 1)

            def split_x(k):
                s = k % 2
                dve.wait_ge(x_high, k + 1)
                if k >= 2:
                    dve.wait_ge(moving_ready, 2 * (k - 1))
                nc.vector.tensor_tensor(x_split[:, s, 1, :], t_ps[:, :],
                                        x_split[:, s, 0, :].bitcast(F32), SUB).then_inc(x_low, 1)

            starts = {first_tile(m + 1) - 1 for m in range(COUPLES)}

            def multiply(g):
                dve.wait_ge(bil_done, g + 1)
                if g >= PROD_SLOTS:
                    dve.wait_ge(summed, (g - PROD_SLOTS) // 2 + 1)
                if 2 * g in starts or 2 * g + 1 in starts:
                    dve.wait_ge(x_ready, max(TILES[2 * g][1], TILES[2 * g + 1][1]) + 1)
                ma, mb = TILES[2 * g][1], TILES[2 * g + 1][1]
                if mb == ma + 1:
                    nc.vector.tensor_tensor(prod[:, g % PROD_SLOTS, :, :], bil[:, g % BIL_SLOTS, :, :],
                                            x_t[:, ma:ma + 2, :], MULT).then_inc(prod_done, 1)
                else:
                    nc.vector.tensor_tensor(prod[:, g % PROD_SLOTS, 0, :], bil[:, g % BIL_SLOTS, 0, :],
                                            x_t[:, ma, :], MULT)
                    nc.vector.tensor_tensor(prod[:, g % PROD_SLOTS, 1, :], bil[:, g % BIL_SLOTS, 1, :],
                                            x_t[:, mb, :], MULT).then_inc(prod_done, 1)

            def finish_block(g):
                dve.wait_ge(summed, BLOCK_ROUNDS * (g + 1))
                if g == 0:
                    dve.wait_ge(weights_in, 16 * 6)
                nc.vector.tensor_tensor(z_t[:, g, :], z_ps[:, :], dense_sb[:, g, :], ADD).then_inc(z_copied, 1)

            for r in range(ROUNDS):
                for q in chunks_at.get(r, []):
                    split_k(q)
                early = [k for k in couples_at.get(r, []) if first_tile(k) // ROUND <= r]
                for k in early:
                    split_x(k)
                multiply(2 * r)
                if r % BLOCK_ROUNDS == 1 and r > 1:
                    finish_block(r // BLOCK_ROUNDS - 1)
                for k in couples_at.get(r, []):
                    if k not in early:
                        split_x(k)
                multiply(2 * r + 1)
            finish_block(BLOCKS - 1)

        @block.tensor
        def _(pe):
            def transpose(k):
                slot = k % X_SLOTS
                pe.wait_ge(gathered[slot], 16 * 2 * BTILES * (k // X_SLOTS + 1))
                if k >= 1:
                    pe.wait_ge(x_ready, k)
                    pe.wait_ge(x_low, k)
                for c in range(BTILES):
                    last = nc.tensor.transpose(t_ps[:, c * P:(c + 1) * P], x_rows[:, slot, c, :], ident[:, :])
                last.then_inc(transposed, 1)

            def contract(g):
                if g >= BIL_SLOTS:
                    pe.wait_ge(prod_done, g - BIL_SLOTS + 1)
                for t in range(2):
                    tile = 2 * g + t
                    j = TILES[tile][0]
                    for part in range(2):
                        last = nc.tensor.matmul(
                            bil[:, g % BIL_SLOTS, t, :], k_st[:, tile // CHUNK % K_SLOTS, tile % CHUNK, :],
                            moving[:, j // 2 % M_SLOTS, j % 2, part, :], start=(part == 0), stop=(part == 1))
                last.then_inc(bil_done, 1)

            def sum_round(r):
                g, s = r // BLOCK_ROUNDS, r % BLOCK_ROUNDS
                pe.wait_ge(prod_done, 2 * r + 2)
                if s == 0 and g >= 1:
                    pe.wait_ge(z_copied, g)
                for c in range(ROUND):
                    last = nc.tensor.matmul(
                        z_ps[c * STRIP:(c + 1) * STRIP, :],
                        pick[:, STRIP - 2 - 2 * s:2 * STRIP - 2 - 2 * s],
                        prod[:, (2 * r + c // 2) % PROD_SLOTS, c % 2, :],
                        start=(s == 0), stop=(s == BLOCK_ROUNDS - 1), tile_position=(0, c * STRIP))
                last.then_inc(summed, 1)

            pe.wait_ge(ident_ready, 1)
            pe.wait_ge(pick_ready, 1)
            ready = 0
            for r in range(ROUNDS):
                for k in couples_at.get(r, []):
                    transpose(k)
                if r % CHUNK_ROUNDS == 0:
                    q = r // CHUNK_ROUNDS
                    pe.wait_ge(k_placed[q % K_SLOTS], 64 * (q // K_SLOTS + 1))
                for g in (2 * r, 2 * r + 1):
                    need = max(TILES[2 * g][0], TILES[2 * g + 1][0]) + 1
                    if need > ready:
                        pe.wait_ge(moving_ready, need)
                        ready = need
                    contract(g)
                if r >= 1:
                    sum_round(r - 1)
            sum_round(ROUNDS - 1)

            pe.wait_ge(weights_in, 16 * 6)
            pe.wait_ge(z_copied, BLOCKS - 1)
            for n in range(H1T):
                cols = slice(n * P, (n + 1) * P)
                for g in range(BLOCKS - 1):
                    nc.tensor.matmul(bil[:, n // 2, n % 2, :], w1_sb[:, g, cols], z_t[:, g, :],
                                     start=(g == 0), stop=False)
            pe.wait_ge(z_copied, BLOCKS)
            for n in range(H1T):
                nc.tensor.matmul(bil[:, n // 2, n % 2, :], w1_sb[:, BLOCKS - 1, n * P:(n + 1) * P],
                                 z_t[:, BLOCKS - 1, :], start=False, stop=True).then_inc(h1_sum, 1)
            for n in range(H1T):
                pe.wait_ge(h1_ready, n + 1)
                for m in range(H2T):
                    last = nc.tensor.matmul(bil[:, 2, m, :], w2_sb[:, n, m * P:(m + 1) * P], h1_t[:, n, :],
                                            start=(n == 0), stop=(n == H1T - 1))
                    if n == H1T - 1:
                        last.then_inc(h2_sum, 1)
            for m in range(H2T):
                pe.wait_ge(h2_ready, m + 1)
                last = nc.tensor.matmul(t_ps[0:1, :], w3_sb[:, m:m + 1], h2_t[:, m, :],
                                        start=(m == 0), stop=(m == H2T - 1))
            last.then_inc(y_sum, 1)


def kernel(**inputs):
    import numpy as np
    import concourse.bacc as bacc
    from concourse.bass_utils import run_bass_kernel_spmd

    first, second = np.triu_indices(FEATURES, k=1)
    pair_of = {(int(i), int(j)): n for n, (i, j) in enumerate(zip(first, second))}
    order = [pair_of.get((2 * m + h, j), PAIRS) for j, m in TILES for h in range(2)]

    weight = np.asarray(inputs["L0_rec_kernel"])
    padded = np.concatenate([weight, np.zeros((EMB, 1, EMB), weight.dtype)], axis=1)[:, order, :]
    kpairs = padded.reshape(EMB, CHUNKS, 2, CHUNK // 2 * P).transpose(1, 2, 0, 3).reshape(
        CHUNKS, P, CHUNK // 2 * P)

    w1 = np.asarray(inputs["W_top1"])
    row_of = np.full((BLOCKS, P), PAIRS)
    for t, (j, m) in enumerate(TILES):
        for h in range(2):
            row_of[z_row(t, h)] = pair_of.get((2 * m + h, j), PAIRS)
    dense_of = np.full((BLOCKS, P), DENSE)
    paddings = [z_row(t, 1) for t, (j, m) in enumerate(TILES) if 2 * m + 1 == j]
    for d, at in enumerate(paddings):
        row_of[at], dense_of[at] = PAIRS + d, d
    w1_rows = w1[row_of]
    dense = np.asarray(inputs["dense_ctx"]).T
    dense_rows = np.concatenate([dense, np.zeros((1, BATCH), dense.dtype)], axis=0)[dense_of]

    ids = np.asarray(inputs["ids"]).reshape(BTILES, P, FEATURES).transpose(1, 0, 2)
    arrays = {
        "ids": ids,
        **{f"tbl_{n}": np.asarray(inputs[f"tbl_{n}"]) for n in range(FEATURES)},
        "kpairs": kpairs,
        "dense_rows": dense_rows.transpose(1, 0, 2),
        "w1": w1_rows.transpose(1, 0, 2),
        "b1": np.asarray(inputs["b_top1"]).reshape(H1T, P).T,
        "w2": np.asarray(inputs["W_top2"]).reshape(H1T, P, H2).transpose(1, 0, 2),
        "b2": np.asarray(inputs["b_top2"]).reshape(H2T, P).T,
        "w3": np.asarray(inputs["W_top3"]).reshape(H2T, P).T,
    }
    nc = bacc.Bacc("TRN2", target_bir_lowering=False, num_devices=1)
    aps = {}
    for name in list(arrays):
        array = np.ascontiguousarray(arrays.pop(name))
        arrays[name + "_dram"] = array
        aps[name] = nc.dram_tensor(name + "_dram", array.shape, mybir.dt.from_np(array.dtype),
                                   kind="ExternalInput").ap()
    out = nc.dram_tensor("out_dram", (BATCH, 1), F32, kind="ExternalOutput").ap()
    build(nc, aps["ids"], [aps[f"tbl_{n}"] for n in range(FEATURES)], aps["kpairs"], aps["dense_rows"], aps["w1"], aps["b1"], aps["w2"], aps["b2"], aps["w3"], out.rearrange("b o -> o b"))
    result = run_bass_kernel_spmd(nc, [arrays], core_ids=[0])
    return result.results[0]["out_dram"]
```

```python
import concourse.bass as bass
from concourse import mybir
from contextlib import ExitStack

F32 = mybir.dt.float32
F32R = mybir.dt.float32r
I32 = mybir.dt.int32
MULT = mybir.AluOpType.mult
ADD = mybir.AluOpType.add
SUB = mybir.AluOpType.subtract
IS_EQUAL = mybir.AluOpType.is_equal
NOT_EQUAL = mybir.AluOpType.not_equal
COPY = mybir.ActivationFunctionType.Copy
RELU = mybir.ActivationFunctionType.Relu

P = 128
FEATURES, EMB, BATCH = 32, 64, 512
BTILES = BATCH // P
COUPLES = FEATURES // 2
TABLE_ROWS = (1000, 1000, 1000, 12500, 125000, 12500, 12500, 1250, 12500, 12500, 12500, 12500, 12500, 12500,
              125000, 1000, 1000, 12500, 1250, 12500, 1250, 12500, 12500, 1250, 12500, 1000, 1000, 1000, 1000,
              1000, 12500, 12500)
HOT_COUPLES = (0, 2)
DUPLICATED = 4
GATHERED = tuple(k for k in range(COUPLES) if k not in HOT_COUPLES)
EARLY_FEATURES = [j for j in range(DUPLICATED) if j // 2 in GATHERED]
ITEMS = [("feature", j) for j in EARLY_FEATURES] + [("couple", k) for k in GATHERED if 2 * k >= DUPLICATED]
HOT = 2 * len(HOT_COUPLES)
HOT_ROWS = 1000
HOT_CHUNKS = 8
HOT_PARTS = HOT_ROWS // HOT_CHUNKS
HOT_FEATURES = [n for n in range(FEATURES) if TABLE_ROWS[n] == HOT_ROWS][:HOT]
COLD_FEATURES = [n for n in range(FEATURES) if n not in HOT_FEATURES]
ORDER = [HOT_FEATURES[2 * HOT_COUPLES.index(k) + h] if k in HOT_COUPLES else
         COLD_FEATURES[2 * GATHERED.index(k) + h] for k in range(COUPLES) for h in range(2)]
TILES = [(j, m) for j in range(1, FEATURES) for m in range((j + 1) // 2)]
NTILES = len(TILES)
ROUND = 4
ROUNDS = NTILES // ROUND
STEPS = NTILES // 2
CHUNK = 16
CHUNKS = NTILES // CHUNK
CHUNK_ROUNDS = CHUNK // ROUND
BLOCK_ROUNDS = P // (2 * ROUND)
BLOCKS = ROUNDS // BLOCK_ROUNDS
STRIP = 32
PAIRS = FEATURES * (FEATURES - 1) // 2
DENSE = 16
H1, H2 = 512, 256
H1T, H2T = H1 // P, H2 // P

X_SLOTS = 4
TABLE_SLOTS = 4
M_SLOTS = 6
HOT_SLOTS = 16
K_SLOTS = 3
PROD_SLOTS = 4
BIL_SLOTS = 3
FIRST_STEPS = 3
AHEAD = 6
POOL_FROM = 10
WEIGHTS_AT = 5


def first_tile(j):
    return j // 2 * ((j + 1) // 2)


def item_step(n):
    kind, i = ITEMS[n]
    j = i if kind == "feature" else 2 * i
    last = i if kind == "feature" else 2 * i + 1
    slot_free = -(-first_tile(max(0, last - M_SLOTS + 1)) // 2)
    ahead = max(0, first_tile(j) - AHEAD) // 2
    return max(slot_free, ahead, item_step(n - 1) + 1 if n else 0)


def items_of(k):
    return [n for n, (kind, i) in enumerate(ITEMS) if (i // 2 if kind == "feature" else i) == k]


def copies_before(n):
    return sum(kind == "couple" for kind, _ in ITEMS[:n])


def position(f):
    return 2 * HOT_COUPLES[f // 2] + f % 2


def chunk_round(q):
    return max(0, CHUNK_ROUNDS * q - 5)


def high_round(q):
    return max(q > 1, chunk_round(q) - 3)


def z_row(tile, second):
    r = tile // ROUND
    return r // BLOCK_ROUNDS, STRIP * (tile % ROUND) + 2 * (r % BLOCK_ROUNDS) + second


def build(nc, ids, ids_hot, tables, kpairs, dense_rows, w1, b1, w2, b2, w3, out):
    items_at, chunks_at, high_at = {}, {}, {}
    for n in range(len(ITEMS)):
        items_at.setdefault(item_step(n), []).append(n)
    for q in range(CHUNKS):
        chunks_at.setdefault(chunk_round(q), []).append(q)
        high_at.setdefault(high_round(q), []).append(q)

    uses = [("hot", k) for k in HOT_COUPLES] + [("tiles", g) for g in range(STEPS)]
    bil_slot = {use: n % BIL_SLOTS for n, use in enumerate(uses)}
    before = {use: uses[n - BIL_SLOTS] for n, use in enumerate(uses) if n >= BIL_SLOTS}

    ctx = ExitStack()
    with ctx:
        def sb(name, shape, dt=F32):
            return ctx.enter_context(nc.sbuf_tensor(name, shape, dt))

        def sem(name):
            return ctx.enter_context(nc.semaphore(name))

        ids_sb = sb("ids_sb", [P, BTILES, FEATURES], I32)
        x_rows = sb("x_rows", [P, X_SLOTS, BTILES, 2 * EMB])
        hot_row = sb("hot_row", [P, HOT_CHUNKS])
        hot_table = sb("hot_table", [P, TABLE_SLOTS, HOT_CHUNKS, 2, EMB], F32R)
        one_hot = sb("one_hot", [P, HOT_SLOTS - 4, BATCH], F32R)
        ident = sb("ident", [P, P])
        x_t = sb("x_t", [P, COUPLES, BATCH])
        x_split = sb("x_split", [P, 2, 2, BATCH], F32R)
        moving = sb("moving", [P, M_SLOTS, 2, BATCH], F32R)
        k_raw = sb("k_raw", [P, 2, CHUNK // 2 * P])
        k_split = sb("k_split", [P, 2, 2, CHUNK // 2 * P], F32R)
        k_st = sb("k_st", [P, K_SLOTS, CHUNK, P], F32R)
        prod = sb("prod", [P, PROD_SLOTS, 2, BATCH])
        pick = sb("pick", [P, 2 * STRIP - 2])
        late = sb("late", [P, 3, BLOCKS, BATCH])
        z_t = late[:, 0, :, :]
        dense_sb = late[:, 1, :, :]
        w1_sb = late[:, 2, :, :]
        b1_sb = sb("b1_sb", [P, H1T])
        w2_sb = sb("w2_sb", [P, H1T, H2])
        b2_sb = sb("b2_sb", [P, H2T])
        w3_sb = sb("w3_sb", [P, H2T, STRIP])
        y_sb = sb("y_sb", [P, P])
        early = late[:, :, :, :].rearrange("p a b n -> p (a b) n")
        hot_ids = early[:, 0:HOT, :].bitcast(I32)
        hot_raw = early[:, HOT:2 * HOT, :].rearrange("p f (c e) -> p f c e", e=EMB)
        one_hots = [one_hot[0:HOT_PARTS, i, :] for i in range(HOT_SLOTS - 4)] + [
            x_split[0:HOT_PARTS, i // 2, i % 2, :] for i in range(4)]
        h2_t = prod[:, 0, :, :]
        h1_t = prod[:, 1:3, :, :].rearrange("p a b n -> p (a b) n")

        bil = ctx.enter_context(nc.psum_tensor("bil", [P, BIL_SLOTS, 2, BATCH], F32))
        z_ps = ctx.enter_context(nc.psum_tensor("z_ps", [P, BATCH], F32))
        def hot_bank(f):
            return z_ps[:, :] if f == HOT - 1 else bil[:, bil_slot["hot", HOT_COUPLES[f // 2]], f % 2, :]

        t_ps = ctx.enter_context(nc.psum_tensor("t_ps", [P, BATCH], F32))

        ids_in = sem("ids_in")
        dense_in = [sem(f"dense_in{g}") for g in range(BLOCKS)]
        weights_in = sem("weights_in")
        zeroed = sem("zeroed")
        pick_zeroed = sem("pick_zeroed")
        ident_ready = sem("ident_ready")
        pick_ready = sem("pick_ready")
        gathered = [[sem(f"gathered{i}_{h}") for h in range(2)] for i in range(X_SLOTS)]
        rows_numbered = sem("rows_numbered")
        hot_ids_in = [sem(f"hot_ids_in{f}") for f in range(HOT)]
        hot_raw_in = [sem(f"hot_raw_in{f}") for f in range(HOT)]
        hot_high = sem("hot_high")
        hot_low = sem("hot_low")
        hot_made = sem("hot_made")
        hot_used = sem("hot_used")
        hot_added = sem("hot_added")
        hot_ready = sem("hot_ready")
        transposed = sem("transposed")
        x_high = sem("x_high")
        x_low = sem("x_low")
        x_ready = sem("x_ready")
        x_copied = sem("x_copied")
        k_in = [sem(f"k_in{i}") for i in range(2)]
        k_high = sem("k_high")
        k_low = sem("k_low")
        k_low_late = sem("k_low_late")
        k_placed = [sem(f"k_placed{i}") for i in range(K_SLOTS)]
        bil_done = sem("bil_done")
        prod_done = sem("prod_done")
        summed = sem("summed")
        z_copied = sem("z_copied")
        h1_sum = sem("h1_sum")
        h1_ready = sem("h1_ready")
        h2_sum = sem("h2_sum")
        h2_ready = sem("h2_ready")
        y_sum = sem("y_sum")
        y_ready = sem("y_ready")
        y_out = sem("y_out")

        block = ctx.enter_context(nc.Block())

        @block.gpsimd
        def _(pool):
            pool.wait_ge(zeroed, 1)
            nc.gpsimd.affine_select(out=ident[:, :], in_=ident[:, :], compare_op=NOT_EQUAL, fill=1.0,
                                    base=0, pattern=[[-1, P]], channel_multiplier=1).then_inc(ident_ready, 1)
            nc.gpsimd.iota(hot_row[0:HOT_PARTS, :], pattern=[[1, HOT_CHUNKS]], base=0,
                           channel_multiplier=HOT_CHUNKS,
                           allow_small_or_imprecise_dtypes=True).then_inc(rows_numbered, 1)
            pool.wait_ge(ids_in, 16)
            for n, k in enumerate(GATHERED):
                if n >= X_SLOTS:
                    pool.wait_ge(transposed, items_of(GATHERED[n - X_SLOTS])[-1] + 1)
                for half in range(2):
                    for c in range(BTILES):
                        nc.gpsimd.indirect_dma_start(
                            x_rows[:, n % X_SLOTS, c, half * EMB:(half + 1) * EMB], None, tables[2 * k + half],
                            bass.IndirectOffsetOnAxis(ap=ids_sb[:, c, 2 * k + half:2 * k + half + 1], axis=0),
                        ).then_inc(gathered[n % X_SLOTS][half], 16)
            for q in range(POOL_FROM, CHUNKS):
                pool.wait_ge(k_high, q + 1)
                nc.gpsimd.tensor_tensor(k_split[:, q % 2, 1, :], k_raw[:, q % 2, :],
                                        k_split[:, q % 2, 0, :].bitcast(F32), SUB).then_inc(k_low_late, 1)

        @block.sync
        def _(sp):
            sp.dma_start(ids_sb[:, :, :], ids).then_inc(ids_in, 16)

            def load_hot(f):
                sp.dma_start(hot_ids[0:HOT_PARTS, f, :],
                             ids_hot[f:f + 1, :].broadcast_to([HOT_PARTS, BATCH])).then_inc(hot_ids_in[f], 16)
                table = tables[position(f)].rearrange("(p c) e -> p c e", c=HOT_CHUNKS)
                sp.dma_start(hot_raw[0:HOT_PARTS, f, :, :], table).then_inc(hot_raw_in[f], 16)

            for f in range(HOT):
                load_hot(f)
                if f == 1:
                    sp.dma_start(k_raw[:, 0, :], kpairs[0, :, :]).then_inc(k_in[0], 16)
            sp.dma_start(k_raw[:, 1, :], kpairs[1, :, :]).then_inc(k_in[1], 16)
            half = CHUNK // 2
            for q in range(CHUNKS):
                if q == WEIGHTS_AT:
                    sp.wait_ge(hot_low, HOT)
                    sp.wait_ge(hot_made, HOT_CHUNKS * HOT)
                if WEIGHTS_AT <= q < WEIGHTS_AT + BLOCKS:
                    g = q - WEIGHTS_AT
                    sp.dma_start(dense_sb[:, g, :], dense_rows[:, g, :]).then_inc(dense_in[g], 16)
                elif WEIGHTS_AT + BLOCKS <= q < WEIGHTS_AT + 2 * BLOCKS:
                    g = q - WEIGHTS_AT - BLOCKS
                    sp.dma_start(w1_sb[:, g, :], w1[:, g, :]).then_inc(weights_in, 16)
                    sp.dma_start(w2_sb[:, g, :], w2[:, g, :]).then_inc(weights_in, 16)
                elif q == WEIGHTS_AT + 2 * BLOCKS:
                    for dst, src in ((b1_sb[:, :], b1), (b2_sb[:, :], b2), (w3_sb[:, :, :], w3)):
                        sp.dma_start(dst, src).then_inc(weights_in, 16)
                sp.wait_ge(k_high, q + 1)
                if q < POOL_FROM:
                    sp.wait_ge(k_low, q + 1)
                else:
                    sp.wait_ge(k_low_late, q - POOL_FROM + 1)
                if q + 2 < CHUNKS:
                    sp.dma_start(k_raw[:, q % 2, :], kpairs[q + 2, :, :]).then_inc(k_in[q % 2], 16)
                if q >= K_SLOTS:
                    sp.wait_ge(bil_done, (q - K_SLOTS + 1) * CHUNK // 2)
                for tiles in range(2):
                    for part in range(2):
                        sp.dma_start(
                            k_st[part * EMB:(part + 1) * EMB, q % K_SLOTS,
                                 tiles * half:(tiles + 1) * half, :].bitcast(F32),
                            k_split[tiles * EMB:(tiles + 1) * EMB, q % 2, part, :].bitcast(F32).rearrange(
                                "p (t n) -> p t n", t=half),
                        ).then_inc(k_placed[q % K_SLOTS], 16)
            sp.wait_ge(y_ready, 1)
            sp.dma_start(out, y_sb[0:P:STRIP, :]).then_inc(y_out, 16)
            sp.wait_ge(y_out, 16)

        @block.scalar
        def _(act):
            def split_k(q):
                act.wait_ge(k_in[q % 2], 16 * (q // 2 + 1))
                if q >= 2:
                    act.wait_ge(k_placed[(q - 2) % K_SLOTS], 64 * ((q - 2) // K_SLOTS + 1))
                nc.scalar.activation(k_split[:, q % 2, 0, :], k_raw[:, q % 2, :], COPY).then_inc(k_high, 1)

            def split_table(f):
                act.wait_ge(hot_raw_in[f], 16)
                if f >= TABLE_SLOTS:
                    act.wait_ge(hot_used, HOT_CHUNKS * (f - TABLE_SLOTS + 1))
                nc.scalar.activation(hot_table[0:HOT_PARTS, f % TABLE_SLOTS, :, 0, :], hot_raw[0:HOT_PARTS, f, :, :],
                                     COPY).then_inc(hot_high, 1)

            def wait_for_slot(j):
                last = j - M_SLOTS
                if last >= 0 and first_tile(last + 1) > 0:
                    act.wait_ge(bil_done, (first_tile(last + 1) - 1) // 2 + 1)
                if last >= 0 and last // 2 in HOT_COUPLES:
                    act.wait_ge(hot_added, 2 * HOT_COUPLES.index(last // 2) + last % 2 + 1)

            def prepare_hot(f):
                j = position(f)
                act.wait_ge(hot_used, HOT_CHUNKS * (f + 1))
                wait_for_slot(j)
                for part in range(2):
                    for copy in range(2):
                        last = nc.scalar.activation(
                            moving[copy * EMB:(copy + 1) * EMB, j % M_SLOTS, part, :],
                            hot_bank(f)[part * EMB:(part + 1) * EMB, :], COPY)
                last.then_inc(hot_ready, 1)

            def prepare_feature(n):
                j = ITEMS[n][1]
                rows = slice(j % 2 * EMB, (j % 2 + 1) * EMB)
                act.wait_ge(transposed, n + 1)
                wait_for_slot(j)
                nc.scalar.activation(moving[:, j % M_SLOTS, 0, :], t_ps[:, :], COPY).then_inc(x_high, 1)
                act.wait_ge(x_low, n + 1)
                nc.scalar.activation(x_t[rows, j // 2, :], t_ps[rows, :], COPY).then_inc(x_ready, 1)

            def prepare_couple(n):
                k = ITEMS[n][1]
                act.wait_ge(transposed, n + 1)
                s = n % 2
                if n >= 2 and ITEMS[n - 2][0] == "couple":
                    act.wait_ge(x_copied, 2 * copies_before(n - 2) + 2)
                nc.scalar.activation(x_split[:, s, 0, :], t_ps[:, :], COPY).then_inc(x_high, 1)
                for feature in range(2):
                    wait_for_slot(2 * k + feature)
                    rows = slice(feature * EMB, (feature + 1) * EMB)
                    for part in range(2):
                        if part == 0:
                            act.wait_ge(x_high, n + 1)
                        else:
                            act.wait_ge(x_low, n + 1)
                        for copy in range(2):
                            last = nc.scalar.activation(
                                moving[copy * EMB:(copy + 1) * EMB, (2 * k + feature) % M_SLOTS, part, :],
                                x_split[rows, s, part, :].bitcast(F32), COPY)
                    last.then_inc(x_copied, 1)
                    if feature == 0:
                        nc.scalar.activation(x_t[:, k, :], t_ps[:, :], COPY).then_inc(x_ready, 1)

            split_table(0)
            split_table(1)
            split_k(0)
            split_table(2)
            split_table(3)
            prepare_hot(0)
            split_k(1)
            prepare_hot(1)
            prepare_feature(0)
            prepare_feature(1)
            prepare_hot(2)
            prepare_hot(3)
            prepare_couple(2)
            split_k(2)
            for g in range(FIRST_STEPS, STEPS):
                if g % 2 == 0:
                    for q in high_at.get(g // 2, []):
                        split_k(q)
                for n in items_at.get(g, []):
                    prepare_couple(n)
            act.wait_ge(weights_in, 16 * (2 * BLOCKS + 3))
            for n in range(H1T):
                act.wait_ge(h1_sum, n + 1)
                nc.scalar.activation(h1_t[:, n, :], bil[:, n // 2, n % 2, :], RELU,
                                     bias=b1_sb[:, n:n + 1]).then_inc(h1_ready, 1)
            for n in range(H2T):
                act.wait_ge(h2_sum, n + 1)
                nc.scalar.activation(h2_t[:, n, :], bil[:, 2, n, :], RELU,
                                     bias=b2_sb[:, n:n + 1]).then_inc(h2_ready, 1)
            act.wait_ge(y_sum, 1)
            nc.scalar.activation(y_sb[:, :], t_ps[:, 0:P], COPY).then_inc(y_ready, 1)

        @block.vector
        def _(dve):
            nc.vector.memset(ident[:, :], 0.0).then_inc(zeroed, 1)
            nc.vector.memset(pick[:, :], 0.0).then_inc(pick_zeroed, 1)
            dve.wait_ge(pick_zeroed, 1)
            nc.vector.memset(pick[0:EMB, STRIP - 2:STRIP - 1], 1.0)
            nc.vector.memset(pick[EMB:P, STRIP - 1:STRIP], 1.0).then_inc(pick_ready, 1)

            def split_k(q):
                dve.wait_ge(k_high, q + 1)
                nc.vector.tensor_tensor(k_split[:, q % 2, 1, :], k_raw[:, q % 2, :],
                                        k_split[:, q % 2, 0, :].bitcast(F32), SUB).then_inc(k_low, 1)

            def split_table(f):
                dve.wait_ge(hot_high, f + 1)
                nc.vector.tensor_tensor(hot_table[0:HOT_PARTS, f % TABLE_SLOTS, :, 1, :],
                                        hot_raw[0:HOT_PARTS, f, :, :],
                                        hot_table[0:HOT_PARTS, f % TABLE_SLOTS, :, 0, :].bitcast(F32),
                                        SUB).then_inc(hot_low, 1)

            def match(f, first, last):
                dve.wait_ge(hot_ids_in[f], 16)
                for c in range(first, last):
                    made = f * HOT_CHUNKS + c
                    if made >= HOT_SLOTS:
                        dve.wait_ge(hot_used, made - HOT_SLOTS + 1)
                    nc.vector.tensor_scalar(one_hots[made % HOT_SLOTS], hot_ids[0:HOT_PARTS, f, :],
                                            hot_row[0:HOT_PARTS, c:c + 1], None, IS_EQUAL).then_inc(hot_made, 1)

            def add_hot(f):
                j = position(f)
                rows = slice(j % 2 * EMB, (j % 2 + 1) * EMB)
                dve.wait_ge(hot_ready, f + 1)
                nc.vector.tensor_tensor(x_t[rows, j // 2, :], moving[EMB:P, j % M_SLOTS, 0, :].bitcast(F32),
                                        moving[EMB:P, j % M_SLOTS, 1, :].bitcast(F32), ADD).then_inc(hot_added, 1)

            def split_x(n):
                kind, i = ITEMS[n]
                dve.wait_ge(x_high, n + 1)
                parts = moving[:, i % M_SLOTS, :, :] if kind == "feature" else x_split[:, n % 2, :, :]
                nc.vector.tensor_tensor(parts[:, 1, :], t_ps[:, :], parts[:, 0, :].bitcast(F32),
                                        SUB).then_inc(x_low, 1)

            starts = {first_tile(2 * m + 2) - 1 for m in range(COUPLES)}

            def multiply(g):
                dve.wait_ge(bil_done, g + 1)
                if g >= PROD_SLOTS:
                    dve.wait_ge(summed, (g - PROD_SLOTS) // 2 + 1)
                for tile in (2 * g, 2 * g + 1):
                    m = TILES[tile][1]
                    if tile in starts:
                        if m in GATHERED:
                            dve.wait_ge(x_ready, items_of(m)[-1] + 1)
                        else:
                            dve.wait_ge(hot_added, 2 * HOT_COUPLES.index(m) + 2)
                slot = bil_slot["tiles", g]
                ma, mb = TILES[2 * g][1], TILES[2 * g + 1][1]
                if mb == ma + 1:
                    nc.vector.tensor_tensor(prod[:, g % PROD_SLOTS, :, :], bil[:, slot, :, :],
                                            x_t[:, ma:ma + 2, :], MULT).then_inc(prod_done, 1)
                else:
                    nc.vector.tensor_tensor(prod[:, g % PROD_SLOTS, 0, :], bil[:, slot, 0, :],
                                            x_t[:, ma, :], MULT)
                    nc.vector.tensor_tensor(prod[:, g % PROD_SLOTS, 1, :], bil[:, slot, 1, :],
                                            x_t[:, mb, :], MULT).then_inc(prod_done, 1)

            def finish_block(g):
                dve.wait_ge(summed, BLOCK_ROUNDS * (g + 1))
                dve.wait_ge(dense_in[g], 16)
                nc.vector.tensor_tensor(z_t[:, g, :], z_ps[:, :], dense_sb[:, g, :], ADD).then_inc(z_copied, 1)

            dve.wait_ge(rows_numbered, 1)
            match(0, 0, 2)
            split_table(0)
            match(0, 2, HOT_CHUNKS)
            split_k(0)
            split_table(1)
            match(1, 0, HOT_CHUNKS)
            add_hot(0)
            split_table(2)
            match(2, 0, HOT_CHUNKS // 2)
            add_hot(1)
            split_x(0)
            match(2, HOT_CHUNKS // 2, HOT_CHUNKS)
            split_x(1)
            split_table(3)
            match(3, 0, HOT_CHUNKS // 2)
            match(3, HOT_CHUNKS // 2, HOT_CHUNKS)
            multiply(0)
            split_k(1)
            multiply(1)
            add_hot(2)
            add_hot(3)
            split_x(2)
            multiply(2)
            for g in range(FIRST_STEPS, STEPS):
                if g % 2 == 0:
                    for q in chunks_at.get(g // 2, []):
                        if 1 < q < POOL_FROM:
                            split_k(q)
                if g % (2 * BLOCK_ROUNDS) == 2:
                    finish_block(g // (2 * BLOCK_ROUNDS) - 1)
                multiply(g)
                for n in items_at.get(g, []):
                    split_x(n)
            finish_block(BLOCKS - 1)

        @block.tensor
        def _(pe):
            def wait_for_banks(*use):
                kind, n = before.get(use, (None, None))
                if kind == "tiles":
                    pe.wait_ge(prod_done, n + 1)
                if kind == "hot":
                    pe.wait_ge(hot_ready, min(HOT - 1, 2 * HOT_COUPLES.index(n) + 2))

            def look_up(f, first=0, last=HOT_CHUNKS):
                if first == 0:
                    pe.wait_ge(hot_low, f + 1)
                    if f % 2 == 0:
                        wait_for_banks("hot", HOT_COUPLES[f // 2])
                for c in range(first, last):
                    made = f * HOT_CHUNKS + c
                    pe.wait_ge(hot_made, made + 1)
                    nc.tensor.matmul(
                        hot_bank(f),
                        hot_table[0:HOT_PARTS, f % TABLE_SLOTS, c, :, :].rearrange("p a e -> p (a e)"),
                        one_hots[made % HOT_SLOTS], start=(c == 0), stop=(c == HOT_CHUNKS - 1),
                    ).then_inc(hot_used, 1)

            def transpose(n):
                kind, i = ITEMS[n]
                k = i // 2 if kind == "feature" else i
                slot = GATHERED.index(k) % X_SLOTS
                for half in [i % 2] if kind == "feature" else [0, 1]:
                    pe.wait_ge(gathered[slot][half], 16 * BTILES * (GATHERED.index(k) // X_SLOTS + 1))
                if n >= 1:
                    pe.wait_ge(x_ready, n)
                for c in range(BTILES):
                    if kind == "feature":
                        for copy in range(2):
                            last = nc.tensor.matmul(
                                t_ps[copy * EMB:(copy + 1) * EMB, c * P:(c + 1) * P],
                                x_rows[:, slot, c, i % 2 * EMB:(i % 2 + 1) * EMB], ident[:, :],
                                tile_position=(0, copy * EMB))
                    else:
                        last = nc.tensor.transpose(t_ps[:, c * P:(c + 1) * P], x_rows[:, slot, c, :], ident[:, :])
                last.then_inc(transposed, 1)

            def contract(g):
                slot = bil_slot["tiles", g]
                wait_for_banks("tiles", g)
                for t in range(2):
                    tile = 2 * g + t
                    j = TILES[tile][0]
                    for part in range(2):
                        last = nc.tensor.matmul(
                            bil[:, slot, t, :], k_st[:, tile // CHUNK % K_SLOTS, tile % CHUNK, :],
                            moving[:, j % M_SLOTS, part, :], start=(part == 0), stop=(part == 1))
                last.then_inc(bil_done, 1)

            def step(g):
                if g % (CHUNK // 2) == 0:
                    q = g // (CHUNK // 2)
                    pe.wait_ge(k_placed[q % K_SLOTS], 64 * (q // K_SLOTS + 1))
                for j in sorted({TILES[2 * g][0], TILES[2 * g + 1][0]}):
                    if first_tile(j) >= 2 * g:
                        if j // 2 in HOT_COUPLES:
                            pe.wait_ge(hot_ready, 2 * HOT_COUPLES.index(j // 2) + j % 2 + 1)
                        elif j < DUPLICATED:
                            pe.wait_ge(x_low, ITEMS.index(("feature", j)) + 1)
                        else:
                            pe.wait_ge(x_copied, 2 * copies_before(ITEMS.index(("couple", j // 2))) + j % 2 + 1)
                contract(g)

            def sum_round(r):
                g, s = r // BLOCK_ROUNDS, r % BLOCK_ROUNDS
                pe.wait_ge(prod_done, 2 * r + 2)
                if r == 0:
                    pe.wait_ge(hot_ready, HOT)
                if s == 0 and g >= 1:
                    pe.wait_ge(z_copied, g)
                for c in range(ROUND):
                    last = nc.tensor.matmul(
                        z_ps[c * STRIP:(c + 1) * STRIP, :],
                        pick[:, STRIP - 2 - 2 * s:2 * STRIP - 2 - 2 * s],
                        prod[:, (2 * r + c // 2) % PROD_SLOTS, c % 2, :],
                        start=(s == 0), stop=(s == BLOCK_ROUNDS - 1), tile_position=(0, c * STRIP))
                last.then_inc(summed, 1)

            pe.wait_ge(ident_ready, 1)
            pe.wait_ge(pick_ready, 1)
            look_up(0)
            look_up(1)
            transpose(0)
            look_up(2, 0, HOT_CHUNKS // 2)
            transpose(1)
            look_up(2, HOT_CHUNKS // 2, HOT_CHUNKS)
            step(0)
            step(1)
            look_up(3)
            step(2)
            transpose(2)
            for g in range(FIRST_STEPS, STEPS):
                for n in items_at.get(g, []):
                    transpose(n)
                step(g)
                if g % 2 == 1:
                    sum_round(g // 2 - 1)
            def sum_ready_blocks(n):
                for g in range(BLOCKS - 1):
                    nc.tensor.matmul(bil[:, n // 2, n % 2, :], w1_sb[:, g, n * P:(n + 1) * P], z_t[:, g, :],
                                     start=(g == 0), stop=False)

            pe.wait_ge(weights_in, 16 * (2 * BLOCKS + 3))
            pe.wait_ge(z_copied, BLOCKS - 1)
            pe.wait_ge(prod_done, STEPS - 2)
            sum_ready_blocks(2)
            sum_ready_blocks(3)
            sum_round(ROUNDS - 1)
            sum_ready_blocks(0)
            sum_ready_blocks(1)
            pe.wait_ge(z_copied, BLOCKS)
            for n in range(H1T):
                nc.tensor.matmul(bil[:, n // 2, n % 2, :], w1_sb[:, BLOCKS - 1, n * P:(n + 1) * P],
                                 z_t[:, BLOCKS - 1, :], start=False, stop=True).then_inc(h1_sum, 1)
            for n in range(H1T):
                pe.wait_ge(h1_ready, n + 1)
                for m in range(H2T):
                    last = nc.tensor.matmul(bil[:, 2, m, :], w2_sb[:, n, m * P:(m + 1) * P], h1_t[:, n, :],
                                            start=(n == 0), stop=(n == H1T - 1))
                    if n == H1T - 1:
                        last.then_inc(h2_sum, 1)
            for m in range(H2T):
                pe.wait_ge(h2_ready, m + 1)
                for c in range(BTILES):
                    last = nc.tensor.matmul(
                        t_ps[c * STRIP:(c + 1) * STRIP, 0:P], w3_sb[:, m, :], h2_t[:, m, c * P:(c + 1) * P],
                        start=(m == 0), stop=(m == H2T - 1), tile_position=(0, c * STRIP))
            last.then_inc(y_sum, 1)


def kernel(**inputs):
    import numpy as np
    import concourse.bacc as bacc
    from concourse.bass_utils import run_bass_kernel_spmd

    first, second = np.triu_indices(FEATURES, k=1)
    number = {(int(i), int(j)): n for n, (i, j) in enumerate(zip(first, second))}

    def pair(tile, h):
        j, m = TILES[tile]
        if 2 * m + h == j:
            return PAIRS, False
        a, b = ORDER[2 * m + h], ORDER[j]
        return number[min(a, b), max(a, b)], b < a

    weight = np.asarray(inputs["L0_rec_kernel"])
    both = np.concatenate([weight.transpose(1, 0, 2), weight.transpose(1, 2, 0),
                           np.zeros((1, EMB, EMB), weight.dtype)])
    pairs = [pair(t, h) for t in range(NTILES) for h in range(2)]
    padded = both[[2 * PAIRS if n == PAIRS else n + PAIRS * turned for n, turned in pairs]].transpose(1, 0, 2)
    kpairs = padded.reshape(EMB, CHUNKS, 2, CHUNK // 2 * P).transpose(1, 2, 0, 3).reshape(
        CHUNKS, P, CHUNK // 2 * P)

    w1 = np.asarray(inputs["W_top1"])
    row_of = np.full((BLOCKS, P), PAIRS)
    for t in range(NTILES):
        for h in range(2):
            row_of[z_row(t, h)] = pair(t, h)[0]
    dense_of = np.full((BLOCKS, P), DENSE)
    paddings = [z_row(t, 1) for t, (j, m) in enumerate(TILES) if 2 * m + 1 == j]
    for d, at in enumerate(paddings):
        row_of[at], dense_of[at] = PAIRS + d, d
    w1_rows = w1[row_of]
    dense = np.asarray(inputs["dense_ctx"]).T
    dense_rows = np.concatenate([dense, np.zeros((1, BATCH), dense.dtype)], axis=0)[dense_of]

    w3 = np.zeros((P, H2T, STRIP), w1.dtype)
    w3[:, :, 0] = np.asarray(inputs["W_top3"]).reshape(H2T, P).T

    ids = np.asarray(inputs["ids"])[:, ORDER]
    arrays = {
        "ids": ids.reshape(BTILES, P, FEATURES).transpose(1, 0, 2),
        "ids_hot": ids[:, [position(f) for f in range(HOT)]].T,
        **{f"tbl_{n}": np.asarray(inputs[f"tbl_{n}"]) for n in range(FEATURES)},
        "kpairs": kpairs,
        "dense_rows": dense_rows.transpose(1, 0, 2),
        "w1": w1_rows.transpose(1, 0, 2),
        "b1": np.asarray(inputs["b_top1"]).reshape(H1T, P).T,
        "w2": np.asarray(inputs["W_top2"]).reshape(H1T, P, H2).transpose(1, 0, 2),
        "b2": np.asarray(inputs["b_top2"]).reshape(H2T, P).T,
        "w3": w3,
    }
    nc = bacc.Bacc("TRN2", target_bir_lowering=False, num_devices=1)
    aps = {}
    for name in list(arrays):
        array = np.ascontiguousarray(arrays.pop(name))
        arrays[name + "_dram"] = array
        aps[name] = nc.dram_tensor(name + "_dram", array.shape, mybir.dt.from_np(array.dtype),
                                   kind="ExternalInput").ap()
    out = nc.dram_tensor("out_dram", (BATCH, 1), F32, kind="ExternalOutput").ap()
    build(nc, aps["ids"], aps["ids_hot"], [aps[f"tbl_{n}"] for n in ORDER], aps["kpairs"], aps["dense_rows"],
          aps["w1"], aps["b1"], aps["w2"], aps["b2"], aps["w3"], out.rearrange("(c b) o -> c (b o)", b=P))
    result = run_bass_kernel_spmd(nc, [arrays], core_ids=[0])
    return result.results[0]["out_dram"]
```
